# Optimizing a Trainium2 kernel written in Bass

```python
import numpy as np
import jax
import jax.numpy as jnp

def _softmax(x, axis=-1):
    return jax.nn.softmax(x, axis=axis)

def _gelu(x):
    return jax.nn.gelu(x, approximate=True)

def _silu(x):
    return jax.nn.silu(x)

def _sigmoid(x):
    return jax.nn.sigmoid(x)

def _layernorm(x, axis=-1, eps=1e-05):
    m = jnp.mean(x, axis=axis, keepdims=True)
    v = jnp.var(x, axis=axis, keepdims=True)
    return (x - m) / jnp.sqrt(v + eps)

def _scatter_add(tgt, idx, src, axis=0):
    return tgt.at[idx].add(src)

def _segment_sum(src, seg, n):
    return jax.ops.segment_sum(src, seg, n)
kernel_name = 'mk_adaln_ffn_d1_seqx_r4_ea4fd5'

def setup_inputs(seed: int=0):
    np.random.seed(seed)
    _w = jnp.asarray

    def _rec_inputs():
        import jax
        import jax.numpy as jnp
        _rk = jax.random.key(seed)
        x = -0.000125 + 0.9999 * jax.random.normal(jax.random.fold_in(_rk, 1), (32, 64, 1024), jnp.float32)
        _lenS = 64 - jax.random.randint(jax.random.fold_in(_rk, 7), (32,), 0, max(1, 64 // 4) + 1, jnp.int32)
        _lenS2 = 64 - jax.random.randint(jax.random.fold_in(_rk, 8), (32,), 0, max(1, 64 // 4) + 1, jnp.int32)
        itok_B_0_7 = jax.random.randint(jax.random.fold_in(_rk, 11), (32,), 0, 8, jnp.int32)
        return (x, itok_B_0_7)
    x, itok_B_0_7 = _rec_inputs()

    def _L0_cond_setup():
        import jax, jax.numpy as jnp
        import numpy as np
        TOP_K = 2
        LANG_BIAS = 5.0
        SCALING = 32.0 / 16.0
        LANGUAGE_PAD_ID = -1
        key = jax.random.key(seed)
        ks = jax.random.split(key, 6)
        B, T, D, O, E, R = (4, 512, 1024, 1024, 8, 16)
        x = jax.random.normal(ks[0], (B, T, D), dtype=jnp.float32)
        language_ids = jax.random.randint(ks[1], (B,), 0, E).astype(jnp.int64)
        W = jax.random.normal(ks[2], (O, D), dtype=jnp.float32) * (1.0 / np.sqrt(D))
        Wr = jax.random.normal(ks[3], (E, D), dtype=jnp.float32) * (1.0 / np.sqrt(D))
        A = jax.random.normal(ks[4], (E, R, D), dtype=jnp.float32) * (1.0 / np.sqrt(D))
        Bm = jax.random.normal(ks[5], (O, R), dtype=jnp.float32) * 0.0
        Bm = jnp.broadcast_to(Bm, (E, O, R)) + jax.random.normal(ks[5], (E, O, R), dtype=jnp.float32) * 0.02
        return {'x': x, 'language_ids': language_ids, 'W': W, 'Wr': Wr, 'A': A, 'B': Bm}
    _L0_cond_all = _L0_cond_setup()
    _L0_cond_in = {k: v for k, v in _L0_cond_all.items() if k in ('W', 'Wr', 'A', 'B')}
    del _L0_cond_all

    def _L0_ffn_setup():
        import jax, jax.numpy as jnp
        import numpy as np
        OUT, IN, RANK = (1024, 1024, 256)
        B, T = (4, 1024)
        key = jax.random.key(seed)
        kx, ku, ks, kv = jax.random.split(key, 4)
        x = jax.random.normal(kx, (B, T, IN), dtype=jnp.float32)
        U = jax.random.normal(ku, (OUT, RANK), dtype=jnp.float32) / np.sqrt(OUT)
        S = jax.random.uniform(ks, (RANK,), dtype=jnp.float32, minval=0.1, maxval=10.0)
        S = jnp.sort(S)[::-1]
        V = jax.random.normal(kv, (IN, RANK), dtype=jnp.float32) / np.sqrt(IN)
        return {'x': x, 'U': U, 'S': S, 'V': V}
    _L0_ffn_all = _L0_ffn_setup()
    _L0_ffn_in = {k: v for k, v in _L0_ffn_all.items() if k in ('U', 'S', 'V')}
    del _L0_ffn_all
    return {'x': x, 'itok_B_0_7': itok_B_0_7, 'L0_cond_W': _L0_cond_in['W'], 'L0_cond_Wr': _L0_cond_in['Wr'], 'L0_cond_A': _L0_cond_in['A'], 'L0_cond_B': _L0_cond_in['B'], 'L0_ffn_U': _L0_ffn_in['U'], 'L0_ffn_S': _L0_ffn_in['S'], 'L0_ffn_V': _L0_ffn_in['V']}

def reference(x, itok_B_0_7, L0_cond_W, L0_cond_Wr, L0_cond_A, L0_cond_B, L0_ffn_U, L0_ffn_S, L0_ffn_V):
    import jax
    import jax.numpy as jnp

    def _L0_cond_ref(x, language_ids, W, Wr, A, B):
        import jax, jax.numpy as jnp
        import numpy as np
        TOP_K = 2
        LANG_BIAS = 5.0
        SCALING = 32.0 / 16.0
        LANGUAGE_PAD_ID = -1
        base = jnp.einsum('btd,od->bto', x, W)
        E = Wr.shape[0]
        logits = jnp.einsum('btd,ed->bte', x.astype(jnp.float32), Wr.astype(jnp.float32))
        expert_targets = language_ids
        valid = expert_targets >= 0
        tgt = jnp.where(valid, expert_targets, 0)
        bias = jax.nn.one_hot(tgt, E, dtype=logits.dtype) * LANG_BIAS
        bias = jnp.where(valid[:, None], bias, 0.0)
        logits = logits + bias[:, None, :]
        topw, topi = jax.lax.top_k(logits, TOP_K)
        weights = jax.nn.softmax(topw, axis=-1)
        gates = jnp.sum(jax.nn.one_hot(topi, E, dtype=weights.dtype) * weights[..., None], axis=-2)
        gates = gates.astype(x.dtype)
        h = jnp.einsum('btd,erd->bter', x, A)
        lora_out = jnp.einsum('bter,bte,eor->bto', h, gates, B)
        return base + SCALING * lora_out

    def _L0_ffn_ref(x, U, S, V):
        import jax, jax.numpy as jnp
        import numpy as np
        OUT, IN, RANK = (1024, 1024, 256)
        B, T = (4, 1024)
        weight = U * S[None, :] @ V.T
        return jnp.einsum('bti,oi->bto', x, weight)
    x = x + _L0_ffn_ref(_L0_cond_ref(x, itok_B_0_7, L0_cond_W, L0_cond_Wr, L0_cond_A, L0_cond_B), L0_ffn_U, L0_ffn_S, L0_ffn_V)
    return x

_drawn_inputs = setup_inputs


def setup_inputs(seed=0):
    import zlib

    import numpy as np

    out = dict(_drawn_inputs(seed))
    spreads = {}
    factors = {'L0_cond_Wr': 4.052}
    for name, (base, spread) in spreads.items():
        noise = np.random.default_rng([zlib.crc32(name.encode()), seed]).standard_normal(out[name].shape)
        drawn = base * np.exp(spread * noise) if base else spread * noise
        out[name] = jnp.asarray(drawn.astype(out[name].dtype))
    for name, factor in factors.items():
        out[name] = (out[name] * factor).astype(out[name].dtype)
    return out
```

```python
from contextlib import ExitStack

import concourse.bass as bass
from concourse import mybir

F32 = mybir.dt.float32
F32R = mybir.dt.float32r
I32 = mybir.dt.int32
U32 = mybir.dt.uint32
ALU = mybir.AluOpType
ACT = mybir.ActivationFunctionType

LANG_BIAS = 5.0
SCALING = 32.0 / 16.0


def adaln_ffn(nc, x, ids, W, Wr, A, B, U, S, V, out):
    P = 128
    NB, SEQ, D = x.shape
    E, R, _ = A.shape
    O, RANK = V.shape
    ER = E * R
    TILES = NB * SEQ // P
    DC = D // P
    OC = O // P
    MC = RANK // P
    BANK = 512
    HALF = D // BANK
    CPB = BANK // P
    LOG = ER
    Z0 = ER + E
    COLS = ER + E + RANK
    RAW = 4
    XSEM = 4
    assert ER == P and P % SEQ == 0 and P // SEQ == 2 and O == D and RANK * 2 == BANK
    assert OC == DC and DC == 2 * CPB and OC % RAW == 0 and TILES % XSEM == 0 and COLS <= BANK

    W_v = W.rearrange("(p k) d -> p k d", k=OC)
    V_v = V.rearrange("(p k) r -> p k r", k=OC)
    B_v = B.rearrange("e (p k) r -> p e (k r)", k=OC)
    A_v = A.rearrange("e r d -> (e r) d")
    U_v = U.rearrange("(t p) r -> p t r", p=P)
    S_v = S.rearrange("(m p o) -> m p o", p=P, o=1)
    x_v = x.rearrange("b t d -> (b t) d").rearrange("(g p) d -> g p d", p=P)
    out_v = out.rearrange("b t d -> (b t) d").rearrange("(g p) d -> g p d", p=P)

    with ExitStack() as ctx:
        def sb(name, shape, dt):
            return ctx.enter_context(nc.sbuf_tensor(name, shape, dt))

        def bank(name):
            return ctx.enter_context(nc.psum_tensor(name, [P, BANK], F32))

        def sem(name):
            return ctx.enter_context(nc.semaphore(name))

        x_all = sb("x_all", [P, TILES, D], F32)
        x_in = sb("x_in", [P, 2, D], F32)
        xT_hi = sb("xT_hi", [P, 2, DC, P], F32R)
        xT_lo = sb("xT_lo", [P, 2, DC, P], F32R)
        raw = sb("raw", [P, RAW, D + RANK], F32)
        w_hi = sb("w_hi", [P, 2, D], F32R)
        w_lo = sb("w_lo", [P, 2, D], F32R)
        v_hi = sb("v_hi", [P, OC, RANK], F32R)
        v_lo = sb("v_lo", [P, OC, RANK], F32R)
        proj_hi = sb("proj_hi", [P, DC, COLS], F32R)
        proj_lo = sb("proj_lo", [P, DC, COLS], F32R)
        us_hi = sb("us_hi", [P, MC, O], F32R)
        us_lo = sb("us_lo", [P, MC, O], F32R)
        bv_hi = sb("bv_hi", [P, RANK], F32R)
        bv_lo = sb("bv_lo", [P, RANK], F32R)
        a_raw = sb("a_raw", [P, D], F32)
        wr_raw = sb("wr_raw", [E, D], F32)
        u_raw = sb("u_raw", [P, O // P, RANK], F32)
        s_col = sb("s_col", [P, MC], F32)
        ident = sb("ident", [P, P], F32)
        zeros = sb("zeros", [P, P], F32R)
        ids_i = sb("ids_i", [P, NB], I32)
        ids_f = sb("ids_f", [P, NB], F32)
        iota_e = sb("iota_e", [P, E], F32)
        target = sb("target", [P, TILES, E], F32)
        logit = sb("logit", [P, E], F32)
        top = sb("top", [P, 8], F32)
        top_i = sb("top_i", [P, 8], U32)
        top_f = sb("top_f", [P, 2], F32)
        dtop = sb("dtop", [P, 2], F32)
        etop = sb("etop", [P, 2], F32)
        esum = sb("esum", [P, 1], F32)
        rsum = sb("rsum", [P, 1], F32)
        wtop = sb("wtop", [P, 2], F32)
        pick = sb("pick", [P, 2, E], F32)
        gate = sb("gate", [P, E], F32)
        gh = sb("gh", [P, ER], F32)
        ghT_hi = sb("ghT_hi", [P, P], F32R)
        ghT_lo = sb("ghT_lo", [P, P], F32R)
        z_sb = sb("z_sb", [P, RANK], F32)
        zT_hi = sb("zT_hi", [P, 2, RANK], F32R)
        zT_lo = sb("zT_lo", [P, 2, RANK], F32R)

        pj = [bank("pj0"), bank("pj1")]
        fin = [bank("fin0"), bank("fin1")]
        tr = [bank("tr0"), bank("tr1")]
        gt = bank("gt")
        zt = bank("zt")
        p_bank = pj + fin
        wrT = gt[:, P:P + DC * E]
        bv_ps = zt[:, RANK:2 * RANK]

        w_load = [sem(f"w_load{j}") for j in range(RAW)]
        a_load = sem("a_load")
        wr_load = sem("wr_load")
        b_load = sem("b_load")
        u_load = sem("u_load")
        s_load = sem("s_load")
        ids_load = sem("ids_load")
        x_load = [sem(f"x_load{j}") for j in range(XSEM)]
        const = sem("const")
        x_in_ready = sem("x_in_ready")
        setup = sem("setup")
        w_hi_done = sem("w_hi_done")
        w_lo_done = sem("w_lo_done")
        w_used = sem("w_used")
        p_hi = sem("p_hi")
        p_lo = sem("p_lo")
        wt_done = sem("wt_done")
        wt_hi = sem("wt_hi")
        wt_lo = sem("wt_lo")
        wr_done = sem("wr_done")
        wr_hi = sem("wr_hi")
        wr_lo = sem("wr_lo")
        bv_done = sem("bv_done")
        bv_hi_done = sem("bv_hi_done")
        bv_lo_done = sem("bv_lo_done")
        xt_done = sem("xt_done")
        xt_hi = sem("xt_hi")
        xt_lo = sem("xt_lo")
        pj_done = sem("pj_done")
        gate_step = sem("gate_step")
        dtop_ready = sem("dtop_ready")
        exp_done = sem("exp_done")
        gh_done = sem("gh_done")
        gt_done = sem("gt_done")
        gt_hi = sem("gt_hi")
        gt_lo = sem("gt_lo")
        z_done = sem("z_done")
        z_copied = sem("z_copied")
        zt_done = sem("zt_done")
        zt_hi = sem("zt_hi")
        zt_lo = sem("zt_lo")
        fin_done = sem("fin_done")
        fin_free = sem("fin_free")
        stored = sem("stored")

        GATE_STEPS = 9

        block = ctx.enter_context(nc.Block())

        @block.sync
        def _(sp):
            def load_w(k):
                if k >= RAW:
                    sp.wait_ge(w_hi_done, k - RAW + 1)
                    sp.wait_ge(w_lo_done, k - RAW + 1)
                sp.dma_start(raw[:, k % RAW, D:D + RANK], V_v[:, k, :]).then_inc(w_load[k % RAW], 16)
                sp.dma_start(raw[:, k % RAW, 0:D], W_v[:, k, :]).then_inc(w_load[k % RAW], 16)

            def load_x(t, j):
                sp.dma_start(x_all[:, t, :], x_v[t, :, :]).then_inc(x_load[j], 16)

            for k in range(RAW):
                load_w(k)
            sp.dma_start(ids_i[:, :], ids.rearrange("(o n) -> o n", o=1).to_broadcast([P, NB])).then_inc(ids_load, 16)
            sp.dma_start(a_raw[:, :], A_v).then_inc(a_load, 16)
            sp.dma_start(wr_raw[:, :], Wr).then_inc(wr_load, 16)
            load_x(0, 0)
            for k in range(RAW, OC):
                load_w(k)
            load_x(1, 1)
            sp.wait_ge(w_hi_done, OC - RAW + 1)
            sp.wait_ge(w_lo_done, OC - RAW + 1)
            sp.dma_start(raw[:, 0, 0:D].rearrange("p (e c) -> p e c", e=E), B_v).then_inc(b_load, 16)
            for m in range(MC):
                sp.dma_start(s_col[:, m:m + 1], S_v[m, :, :]).then_inc(s_load, 16)
            sp.dma_start(u_raw[:, :, :], U_v).then_inc(u_load, 16)
            for j in range(2, XSEM):
                load_x(j, j)
            with sp.Fori(1, TILES // XSEM) as i:
                for j in range(XSEM):
                    sp.wait_ge(x_load[j], 16 * i)
                    load_x(XSEM * i + j, j)
            with sp.Fori(0, TILES) as t:
                sp.wait_ge(fin_free, HALF * t + 2 * HALF)
                sp.dma_start(out_v[t, :, :], x_all[:, t, :]).then_inc(stored, 16)
            sp.wait_ge(stored, 16 * TILES)

        @block.gpsimd
        def _(pool):
            nc.gpsimd.memset(zeros[:, :].bitcast(F32), 0.0).then_inc(const, 1)
            nc.gpsimd.memset(ident[:, :], 0.0).then_inc(const, 1)
            pool.wait_ge(const, 2)
            nc.gpsimd.affine_select(out=ident[:, :], in_=ident[:, :], compare_op=ALU.not_equal, fill=1.0,
                                    base=0, pattern=[[-1, P]], channel_multiplier=1).then_inc(const, 1)
            for e in range(E):
                nc.gpsimd.memset(iota_e[:, e:e + 1], float(e)).then_inc(const, 1)

            def place_x(t, i, j):
                pool.wait_ge(x_load[j], 16 * i + 16)
                pool.wait_ge(const, 3)
                nc.gpsimd.tensor_copy(x_in[:, j % 2, :], x_all[:, t, :]).then_inc(x_in_ready, 1)

            for j in range(XSEM):
                if j >= 2:
                    pool.wait_ge(xt_done, 2 * (j - 2) + 2)
                place_x(j, 0, j)
            with pool.Fori(1, TILES // XSEM) as i:
                for j in range(XSEM):
                    pool.wait_ge(xt_done, 2 * (XSEM * i + j - 2) + 2)
                    place_x(XSEM * i + j, i, j)

        @block.tensor
        def _(pe):
            def triple(dst, l_hi, l_lo, r_hi, r_lo, first, last, shared=False):
                nc.tensor.matmul(dst, l_hi, r_hi, start=first, stop=False, skip_group_check=shared)
                nc.tensor.matmul(dst, l_hi, r_lo, start=False, stop=False, skip_group_check=shared)
                return nc.tensor.matmul(dst, l_lo, r_hi, start=False, stop=last, skip_group_check=shared)

            def transpose_x(t, q, b):
                if b == 0:
                    pe.wait_ge(x_in_ready, t + 1)
                for c in range(CPB):
                    k = CPB * b + c
                    last = nc.tensor.transpose(tr[b][:, c * P:(c + 1) * P], x_in[:, q, k * P:(k + 1) * P], ident[:, :])
                last.then_inc(xt_done, 1)

            def p_chunk(k, j):
                pe.wait_ge(w_lo_done, k + 1)
                for m in range(DC):
                    cols = slice(m * P, (m + 1) * P)
                    h = slice(RANK * (m % 2), RANK * (m % 2 + 1))
                    last = triple(p_bank[m // 2][:, h], w_hi[:, j % 2, cols], w_lo[:, j % 2, cols],
                                  v_hi[:, k, :], v_lo[:, k, :], False, True, shared=True)
                return last

            def project(t, q, k):
                xk = (xT_hi[:, q, k, :], xT_lo[:, q, k, :])
                return triple(pj[q][:, 0:COLS], *xk, proj_hi[:, k, :], proj_lo[:, k, :], k == 0, k == DC - 1)

            def step(s, q, has_project=True, has_transpose=True, has_mix=True, has_expand=True):
                if has_project:
                    if s is not 0 and s is not 1:
                        pe.wait_ge(z_copied, s - 1)
                    for k in range(DC):
                        if k % CPB == 0:
                            pe.wait_ge(xt_lo, 2 * s + k // CPB + 1)
                        if s is 0 and k % 2 == 0:
                            pe.wait_ge(*((p_lo, k // 2 + 1) if k < 4 else (fin_free, k // 2 - 1)))
                        last = project(s, q, k)
                        if has_transpose and k in (0, 2):
                            b = k // 2
                            if b == 1:
                                pe.wait_ge(xt_lo, 2 * s + 2)
                            if s is 1:
                                pe.wait_ge(wt_lo, 6)
                            transpose_x(s + 1, 1 - q, b)
                        if has_mix and k == CPB - 1:
                            transpose_gh(s - 1)
                    last.then_inc(pj_done, 1)
                elif has_mix:
                    transpose_gh(s - 1)
                if has_mix:
                    pe.wait_ge(gt_lo, s)
                    triple(pj[1 - q][:, Z0:COLS], ghT_hi[:, :], ghT_lo[:, :], bv_hi[:, :], bv_lo[:, :],
                           False, True, shared=True).then_inc(z_done, 1)
                if has_expand:
                    pe.wait_ge(zt_lo, s - 1)
                    expand(s - 2, q, 0)
                if has_mix:
                    pe.wait_ge(z_copied, s)
                    if s is not 1:
                        pe.wait_ge(zt_lo, s - 1)
                    for m in range(MC):
                        last = nc.tensor.transpose(zt[:, m * P:(m + 1) * P], z_sb[:, m * P:(m + 1) * P], ident[:, :])
                    last.then_inc(zt_done, 1)
                if has_expand:
                    expand(s - 2, q, 1)

            def transpose_gh(t):
                pe.wait_ge(gh_done, t + 1)
                nc.tensor.transpose(gt[:, 0:P], gh[:, :], ident[:, :]).then_inc(gt_done, 1)

            def expand(t, q, n):
                pe.wait_ge(fin_free, HALF * t + n + 1)
                for m in range(MC):
                    zk = slice(m * P, (m + 1) * P)
                    o = slice(n * BANK, (n + 1) * BANK)
                    last = triple(fin[n][:, :], zT_hi[:, q, zk], zT_lo[:, q, zk], us_hi[:, m, o], us_lo[:, m, o],
                                  m == 0, m == MC - 1)
                last.then_inc(fin_done, 1)

            pe.wait_ge(const, 3 + E)
            zero_row = zeros[:, :].rearrange("p (o n) -> p o n", o=1).to_broadcast([P, CPB, P])
            for b in range(4):
                last = nc.tensor.matmul(p_bank[b][:, :].rearrange("p (c n) -> p c n", c=CPB), zeros[:, :], zero_row,
                                        start=True, stop=True)
                if b >= 2:
                    last.then_inc(w_used, 1)
            with pe.Fori(0, OC // RAW) as i:
                for j in range(RAW):
                    p_chunk(RAW * i + j, j).then_inc(w_used, 1)

            pe.wait_ge(wr_load, 16)
            for k in range(DC):
                last = nc.tensor.transpose(wrT[:, k * E:(k + 1) * E], wr_raw[:, k * P:(k + 1) * P], ident[0:E, 0:E])
            last.then_inc(wr_done, 1)
            pe.wait_ge(a_load, 16)
            for b in range(2):
                for c in range(CPB):
                    k = CPB * b + c
                    last = nc.tensor.transpose(tr[b][:, c * P:(c + 1) * P], a_raw[:, k * P:(k + 1) * P], ident[:, :])
                last.then_inc(wt_done, 1)
            pe.wait_ge(w_lo_done, OC + 1)
            for k in range(OC):
                cols = slice(k * ER, (k + 1) * ER)
                last = triple(bv_ps, w_hi[:, 0, cols], w_lo[:, 0, cols], v_hi[:, k, :], v_lo[:, k, :],
                              k == 0, k == OC - 1)
                if k in (3, 5):
                    pe.wait_ge(wt_lo, (k - 1) // 2)
                    transpose_x(0, 0, (k - 3) // 2)
            last.then_inc(bv_done, 1)

            step(0, 0, has_mix=False, has_expand=False)
            pe.wait_ge(u_load, 16)
            for m in range(MC):
                for b in range(2):
                    if m == 0:
                        pe.wait_ge(xt_lo, 2 + b + 1)
                    else:
                        pe.wait_ge(wt_lo, 2 + b + 1)
                    for c in range(CPB):
                        last = nc.tensor.transpose(tr[b][:, c * P:(c + 1) * P],
                                                   u_raw[:, CPB * b + c, m * P:(m + 1) * P], ident[:, :])
                    last.then_inc(wt_done, 1)
            pe.wait_ge(bv_lo_done, 1)
            step(1, 1, has_expand=False)
            with pe.Fori(1, TILES // 2 - 1) as i:
                for q in range(2):
                    step(2 * i + q, q)
            step(TILES - 2, 0)
            step(TILES - 1, 1, has_transpose=False)
            step(TILES, 0, has_project=False, has_transpose=False)
            step(TILES + 1, 1, has_project=False, has_transpose=False, has_mix=False)

        @block.scalar
        def _(act):
            def split_x(t, q):
                for b in range(2):
                    act.wait_ge(xt_done, 2 * t + b + 1)
                    nc.scalar.copy(xT_hi[:, q, CPB * b:CPB * (b + 1), :],
                                   tr[b][:, :].rearrange("p (c n) -> p c n", c=CPB)).then_inc(xt_hi, 1)

            def step(s, q, has_project=True, has_transpose=True, has_mix=True):
                if has_transpose:
                    split_x(s + 1, 1 - q)
                if has_mix:
                    act.wait_ge(gt_done, s)
                    nc.scalar.copy(ghT_hi[:, :], gt[:, 0:P]).then_inc(gt_hi, 1)
                    act.wait_ge(z_done, s)
                    nc.scalar.copy(z_sb[:, :], pj[1 - q][:, Z0:COLS]).then_inc(z_copied, 1)
                if has_project:
                    act.wait_ge(dtop_ready, s + 1)
                    nc.scalar.activation(etop[:, :], dtop[:, :], ACT.Exp, accum_out=esum[:, :]).then_inc(exp_done, 1)
                if has_mix:
                    act.wait_ge(zt_done, s)
                    nc.scalar.copy(zT_hi[:, 1 - q, :], zt[:, 0:RANK]).then_inc(zt_hi, 1)

            with act.Fori(0, OC // RAW) as i:
                for j in range(RAW):
                    act.wait_ge(w_load[j], 32 * i + 32)
                    act.wait_ge(w_used, RAW * i + j + 1)
                    nc.scalar.copy(w_hi[:, j % 2, :], raw[:, j, 0:D])
                    nc.scalar.copy(v_hi[:, RAW * i + j, :], raw[:, j, D:D + RANK]).then_inc(w_hi_done, 1)
            act.wait_ge(b_load, 16)
            act.wait_ge(w_used, OC + 1)
            nc.scalar.copy(w_hi[:, 0, :].rearrange("p (k e r) -> p k e r", k=OC, e=E),
                           raw[:, 0, 0:D].rearrange("p (e k r) -> p k e r", e=E, k=OC)).then_inc(w_hi_done, 1)
            act.wait_ge(wr_done, 1)
            nc.scalar.copy(proj_hi[:, :, LOG:LOG + E], wrT.rearrange("p (k e) -> p k e", k=DC)).then_inc(wr_hi, 1)
            for b in range(2):
                act.wait_ge(wt_done, b + 1)
                nc.scalar.copy(proj_hi[:, CPB * b:CPB * (b + 1), 0:ER],
                               tr[b][:, :].rearrange("p (c n) -> p c n", c=CPB)).then_inc(wt_hi, 1)
            act.wait_ge(w_used, OC + 2)
            for b in range(4):
                if b == 1:
                    split_x(0, 0)
                nc.scalar.copy(proj_hi[:, 2 * b:2 * b + 2, Z0:COLS],
                               p_bank[b][:, :].rearrange("p (c n) -> p c n", c=2)).then_inc(p_hi, 1)
            act.wait_ge(bv_done, 1)
            nc.scalar.copy(bv_hi[:, :], bv_ps).then_inc(bv_hi_done, 1)
            step(0, 0, has_mix=False)
            act.wait_ge(s_load, 16 * MC)
            for m in range(MC):
                for b in range(2):
                    act.wait_ge(wt_done, 2 + 2 * m + b + 1)
                    nc.scalar.activation(us_hi[:, m, b * BANK:(b + 1) * BANK], tr[b][:, :], ACT.Copy,
                                         scale=s_col[:, m:m + 1]).then_inc(wt_hi, 1)
            step(1, 1)
            with act.Fori(1, TILES // 2 - 1) as i:
                for q in range(2):
                    step(2 * i + q, q)
            step(TILES - 2, 0)
            step(TILES - 1, 1, has_transpose=False)
            step(TILES, 0, has_project=False, has_transpose=False)

        @block.vector
        def _(dve):
            def split_x(t, q):
                for b in range(2):
                    dve.wait_ge(xt_hi, 2 * t + b + 1)
                    blocks = slice(CPB * b, CPB * (b + 1))
                    nc.vector.tensor_sub(xT_lo[:, q, blocks, :], tr[b][:, :].rearrange("p (c n) -> p c n", c=CPB),
                                         xT_hi[:, q, blocks, :].bitcast(F32)).then_inc(xt_lo, 1)

            def gates_top(s, q):
                n = GATE_STEPS * s
                dve.wait_ge(pj_done, s + 1)
                nc.vector.scalar_tensor_tensor(logit[:, :], target[:, s, :], LANG_BIAS, pj[q][:, LOG:LOG + E],
                                               ALU.mult, ALU.add).then_inc(gate_step, 1)
                nc.vector.drain()
                nc.vector.max(top[:, :], logit[:, :]).then_inc(gate_step, 1)
                nc.vector.drain()
                nc.vector.tensor_scalar(dtop[:, :], top[:, 0:2], top[:, 0:1], None, ALU.subtract).then_inc(dtop_ready, 1)
                nc.vector.max_index(top_i[:, :], top[:, :], logit[:, :]).then_inc(gate_step, 1)
                dve.wait_ge(gate_step, n + 3)
                nc.vector.tensor_copy(top_f[:, :], top_i[:, 0:2]).then_inc(gate_step, 1)

            def gates_apply(s, q):
                n = GATE_STEPS * s
                dve.wait_ge(exp_done, s + 1)
                nc.vector.reciprocal(rsum[:, :], esum[:, :]).then_inc(gate_step, 1)
                dve.wait_ge(gate_step, n + 5)
                nc.vector.tensor_scalar(wtop[:, :], etop[:, :], rsum[:, :], SCALING, ALU.mult, ALU.mult).then_inc(gate_step, 1)
                dve.wait_ge(gate_step, n + 6)
                for j in range(2):
                    nc.vector.tensor_scalar(pick[:, j, :], iota_e[:, :], top_f[:, j:j + 1], wtop[:, j:j + 1],
                                            ALU.is_equal, ALU.mult).then_inc(gate_step, 1)
                dve.wait_ge(gate_step, n + 8)
                nc.vector.tensor_add(gate[:, :], pick[:, 0, :], pick[:, 1, :]).then_inc(gate_step, 1)
                dve.wait_ge(gate_step, n + 9)
                nc.vector.tensor_tensor(gh[:, :].rearrange("p (e r) -> p e r", e=E),
                                        pj[q][:, 0:ER].rearrange("p (e r) -> p e r", e=E),
                                        gate[:, :].rearrange("p (e o) -> p e o", o=1).to_broadcast([P, E, R]),
                                        ALU.mult).then_inc(gh_done, 1)

            def residual(t, n):
                cols = slice(n * BANK, (n + 1) * BANK)
                dve.wait_ge(fin_done, HALF * t + n + 1)
                nc.vector.tensor_add(x_all[:, t, cols], fin[n][:, :], x_all[:, t, cols]).then_inc(fin_free, 1)

            def step(s, q, has_project=True, has_transpose=True, has_mix=True, has_expand=True):
                if has_transpose:
                    split_x(s + 1, 1 - q)
                if has_mix:
                    dve.wait_ge(gt_hi, s)
                    nc.vector.tensor_sub(ghT_lo[:, :], gt[:, 0:P], ghT_hi[:, :].bitcast(F32)).then_inc(gt_lo, 1)
                if has_project:
                    gates_top(s, q)
                if has_expand:
                    residual(s - 2, 0)
                if has_mix:
                    dve.wait_ge(zt_hi, s)
                    nc.vector.tensor_sub(zT_lo[:, 1 - q, :], zt[:, 0:RANK],
                                         zT_hi[:, 1 - q, :].bitcast(F32)).then_inc(zt_lo, 1)
                if has_project:
                    gates_apply(s, q)
                if has_expand:
                    residual(s - 2, 1)

            with dve.Fori(0, OC // RAW) as i:
                for j in range(RAW):
                    k = RAW * i + j
                    dve.wait_ge(w_hi_done, k + 1)
                    nc.vector.tensor_sub(w_lo[:, j % 2, :], raw[:, j, 0:D], w_hi[:, j % 2, :].bitcast(F32))
                    nc.vector.tensor_sub(v_lo[:, k, :], raw[:, j, D:D + RANK],
                                         v_hi[:, k, :].bitcast(F32)).then_inc(w_lo_done, 1)
            dve.wait_ge(ids_load, 16)
            dve.wait_ge(const, 3 + E)
            nc.vector.tensor_copy(ids_f[:, :], ids_i[:, :]).then_inc(setup, 1)
            dve.wait_ge(setup, 1)
            for h in range(2):
                rows = slice(h * SEQ, (h + 1) * SEQ)
                nc.vector.tensor_tensor(
                    target[rows, :, :],
                    ids_f[rows, h:NB:2].rearrange("p (t o) -> p t o", o=1).to_broadcast([SEQ, TILES, E]),
                    iota_e[rows, :].rearrange("p (o e) -> p o e", o=1).to_broadcast([SEQ, TILES, E]),
                    ALU.is_equal).then_inc(setup, 1)
            dve.wait_ge(setup, 3)
            dve.wait_ge(w_hi_done, OC + 1)
            nc.vector.tensor_sub(w_lo[:, 0, :].rearrange("p (k e r) -> p k e r", k=OC, e=E),
                                 raw[:, 0, 0:D].rearrange("p (e k r) -> p k e r", e=E, k=OC),
                                 w_hi[:, 0, :].bitcast(F32).rearrange("p (k e r) -> p k e r", k=OC, e=E)
                                 ).then_inc(w_lo_done, 1)
            dve.wait_ge(wr_hi, 1)
            nc.vector.tensor_sub(proj_lo[:, :, LOG:LOG + E], wrT.rearrange("p (k e) -> p k e", k=DC),
                                 proj_hi[:, :, LOG:LOG + E].bitcast(F32)).then_inc(wr_lo, 1)
            for b in range(2):
                dve.wait_ge(wt_hi, b + 1)
                blocks = slice(CPB * b, CPB * (b + 1))
                nc.vector.tensor_sub(proj_lo[:, blocks, 0:ER], tr[b][:, :].rearrange("p (c n) -> p c n", c=CPB),
                                     proj_hi[:, blocks, 0:ER].bitcast(F32)).then_inc(wt_lo, 1)
            for b in range(4):
                if b == 1:
                    split_x(0, 0)
                dve.wait_ge(p_hi, b + 1)
                nc.vector.tensor_sub(proj_lo[:, 2 * b:2 * b + 2, Z0:COLS],
                                     p_bank[b][:, :].rearrange("p (c n) -> p c n", c=2),
                                     proj_hi[:, 2 * b:2 * b + 2, Z0:COLS].bitcast(F32)).then_inc(p_lo if b < 2 else fin_free, 1)
            dve.wait_ge(bv_hi_done, 1)
            nc.vector.tensor_sub(bv_lo[:, :], bv_ps, bv_hi[:, :].bitcast(F32)).then_inc(bv_lo_done, 1)
            step(0, 0, has_mix=False, has_expand=False)
            for m in range(MC):
                for b in range(2):
                    cols = slice(b * BANK, (b + 1) * BANK)
                    dve.wait_ge(wt_hi, 2 + 2 * m + b + 1)
                    nc.vector.scalar_tensor_tensor(us_lo[:, m, cols], tr[b][:, :], s_col[:, m:m + 1],
                                                   us_hi[:, m, cols].bitcast(F32), ALU.mult,
                                                   ALU.subtract).then_inc(wt_lo, 1)
            step(1, 1, has_expand=False)
            with dve.Fori(1, TILES // 2 - 1) as i:
                for q in range(2):
                    step(2 * i + q, q)
            step(TILES - 2, 0)
            step(TILES - 1, 1, has_transpose=False)
            step(TILES, 0, has_project=False, has_transpose=False)
            step(TILES + 1, 1, has_project=False, has_transpose=False, has_mix=False)


INPUTS = ['x', 'itok_B_0_7', 'L0_cond_W', 'L0_cond_Wr', 'L0_cond_A', 'L0_cond_B', 'L0_ffn_U', 'L0_ffn_S', 'L0_ffn_V']


def kernel(**inputs):
    import numpy as np
    import concourse.bacc as bacc
    from concourse.bass_utils import run_bass_kernel_spmd

    nc = bacc.Bacc("TRN2", target_bir_lowering=False, num_devices=1)
    arrays, args = {}, []
    for name in INPUTS:
        a = np.ascontiguousarray(inputs[name])
        arrays["in_" + name] = a
        args.append(nc.dram_tensor("in_" + name, a.shape, mybir.dt.from_np(a.dtype), kind="ExternalInput").ap())
    out = nc.dram_tensor("out", inputs["x"].shape, F32, kind="ExternalOutput")
    adaln_ffn(nc, *args, out.ap())
    result = run_bass_kernel_spmd(nc, [arrays], core_ids=[0])
    return result.results[0]["out"]
```

```python
from contextlib import ExitStack

import concourse.bass as bass
from concourse import mybir

F32 = mybir.dt.float32
F32R = mybir.dt.float32r
I32 = mybir.dt.int32
U32 = mybir.dt.uint32
ALU = mybir.AluOpType
ACT = mybir.ActivationFunctionType

LANG_BIAS = 5.0
SCALING = 32.0 / 16.0


def adaln_ffn(nc, x, ids, W, Wr, A, B, U, S, V, out):
    P = 128
    NB, SEQ, D = x.shape
    E, R, _ = A.shape
    O, RANK = V.shape
    ER = E * R
    TILES = NB * SEQ // P
    DC = D // P
    OC = O // P
    MC = RANK // P
    BANK = 512
    HALF = D // BANK
    CPB = BANK // P
    LOG = ER
    Z0 = ER + E
    COLS = ER + E + RANK
    RAW = 4
    XSEM = 4
    WH = D // 2
    HPC = 2
    ZERO_ROUNDS = 4
    assert ER == P and P % SEQ == 0 and P // SEQ == 2 and O == D and RANK * 2 == BANK
    assert OC == DC and DC == 2 * CPB and OC % RAW == 0 and TILES % XSEM == 0 and COLS <= BANK

    W_v = W.rearrange("(p k) d -> p k d", k=OC)
    V_v = V.rearrange("(p k) r -> p k r", k=OC)
    B_v = B.rearrange("e (p k) r -> p e (k r)", k=OC)
    A_v = A.rearrange("e r d -> (e r) d")
    U_v = U.rearrange("(t p) r -> p t r", p=P)
    S_v = S.rearrange("(m p o) -> m p o", p=P, o=1)
    x_v = x.rearrange("b t d -> (b t) d").rearrange("(g p) d -> g p d", p=P)
    out_v = out.rearrange("b t d -> (b t) d").rearrange("(g p) d -> g p d", p=P)

    with ExitStack() as ctx:
        def sb(name, shape, dt):
            return ctx.enter_context(nc.sbuf_tensor(name, shape, dt))

        def bank(name):
            return ctx.enter_context(nc.psum_tensor(name, [P, BANK], F32))

        def sem(name):
            return ctx.enter_context(nc.semaphore(name))

        x_all = sb("x_all", [P, TILES, D], F32)
        x_in = sb("x_in", [P, 2, D], F32)
        xT_hi = sb("xT_hi", [P, 2, DC, P], F32R)
        xT_lo = sb("xT_lo", [P, 2, DC, P], F32R)
        raw = sb("raw", [P, RAW, D + RANK], F32)
        w_hi = sb("w_hi", [P, 2, D], F32R)
        w_lo = sb("w_lo", [P, 2, D], F32R)
        v_hi = sb("v_hi", [P, OC, RANK], F32R)
        v_lo = sb("v_lo", [P, OC, RANK], F32R)
        proj_hi = sb("proj_hi", [P, DC, COLS], F32R)
        proj_lo = sb("proj_lo", [P, DC, COLS], F32R)
        us_hi = sb("us_hi", [P, MC, O], F32R)
        us_lo = sb("us_lo", [P, MC, O], F32R)
        bv_hi = sb("bv_hi", [P, RANK], F32R)
        bv_lo = sb("bv_lo", [P, RANK], F32R)
        a_raw = sb("a_raw", [P, D], F32)
        wr_raw = sb("wr_raw", [E, D], F32)
        u_raw = sb("u_raw", [P, O // P, RANK], F32)
        s_col = sb("s_col", [P, MC], F32)
        ident = sb("ident", [P, P], F32)
        zeros = sb("zeros", [P, P], F32R)
        ids_i = sb("ids_i", [P, NB], I32)
        ids_f = sb("ids_f", [P, NB], F32)
        iota_e = sb("iota_e", [P, E], F32)
        target = sb("target", [P, TILES, E], F32)
        logit = sb("logit", [P, E], F32)
        top = sb("top", [P, 8], F32)
        top_i = sb("top_i", [P, 8], U32)
        top_f = sb("top_f", [P, 2], F32)
        dtop = sb("dtop", [P, 2], F32)
        etop = sb("etop", [P, 2], F32)
        esum = sb("esum", [P, 1], F32)
        rsum = sb("rsum", [P, 1], F32)
        wtop = sb("wtop", [P, 2], F32)
        pick = sb("pick", [P, 2, E], F32)
        gate = sb("gate", [P, E], F32)
        gh = sb("gh", [P, ER], F32)
        ghT_hi = sb("ghT_hi", [P, P], F32R)
        ghT_lo = sb("ghT_lo", [P, P], F32R)
        z_sb = sb("z_sb", [P, RANK], F32)
        zT_hi = sb("zT_hi", [P, 2, RANK], F32R)
        zT_lo = sb("zT_lo", [P, 2, RANK], F32R)

        pj = [bank("pj0"), bank("pj1")]
        fin = [bank("fin0"), bank("fin1")]
        tr = [bank("tr0"), bank("tr1")]
        gt = bank("gt")
        zt = bank("zt")
        p_bank = pj + fin
        wrT = gt[:, P:P + DC * E]
        bv_ps = zt[:, RANK:2 * RANK]

        va_load = [sem(f"va_load{j}") for j in range(RAW)]
        wb_load = [sem(f"wb_load{j}") for j in range(RAW)]
        a_load = sem("a_load")
        wr_load = sem("wr_load")
        b_load = sem("b_load")
        u_load = sem("u_load")
        s_load = sem("s_load")
        ids_load = sem("ids_load")
        x_load = [sem(f"x_load{j}") for j in range(XSEM)]
        act_warm = sem("act_warm")
        const = sem("const")
        x_in_ready = sem("x_in_ready")
        setup = sem("setup")
        w_hi_done = sem("w_hi_done")
        w_lo_done = sem("w_lo_done")
        w_used = sem("w_used")
        p_hi = sem("p_hi")
        p_lo = sem("p_lo")
        wt_done = sem("wt_done")
        wt_hi = sem("wt_hi")
        wt_lo = sem("wt_lo")
        wr_done = sem("wr_done")
        wr_hi = sem("wr_hi")
        wr_lo = sem("wr_lo")
        bv_done = sem("bv_done")
        bv_hi_done = sem("bv_hi_done")
        bv_lo_done = sem("bv_lo_done")
        xt_done = sem("xt_done")
        xt_hi = sem("xt_hi")
        xt_lo = sem("xt_lo")
        pj_done = sem("pj_done")
        gate_step = sem("gate_step")
        dtop_ready = sem("dtop_ready")
        exp_done = sem("exp_done")
        gh_done = sem("gh_done")
        gt_done = sem("gt_done")
        gt_hi = sem("gt_hi")
        gt_lo = sem("gt_lo")
        z_done = sem("z_done")
        z_copied = sem("z_copied")
        zt_done = sem("zt_done")
        zt_hi = sem("zt_hi")
        zt_lo = sem("zt_lo")
        fin_done = sem("fin_done")
        fin_free = sem("fin_free")
        stored = sem("stored")

        GATE_STEPS = 9

        block = ctx.enter_context(nc.Block())

        @block.sync
        def _(sp):
            def load_w(k):
                if k >= RAW:
                    sp.wait_ge(w_lo_done, HPC * (k - RAW) + HPC)
                sp.dma_start(raw[:, k % RAW, D:D + RANK], V_v[:, k, :]).then_inc(va_load[k % RAW], 16)
                sp.dma_start(raw[:, k % RAW, 0:WH], W_v[:, k, 0:WH]).then_inc(va_load[k % RAW], 16)
                sp.dma_start(raw[:, k % RAW, WH:D], W_v[:, k, WH:D]).then_inc(wb_load[k % RAW], 16)

            def load_x(t, j):
                sp.dma_start(x_all[:, t, :], x_v[t, :, :]).then_inc(x_load[j], 16)

            for k in range(RAW):
                load_w(k)
            sp.dma_start(ids_i[:, :], ids.rearrange("(o n) -> o n", o=1).to_broadcast([P, NB])).then_inc(ids_load, 16)
            sp.dma_start(a_raw[:, :], A_v).then_inc(a_load, 16)
            sp.dma_start(wr_raw[:, :], Wr).then_inc(wr_load, 16)
            load_x(0, 0)
            for k in range(RAW, OC):
                load_w(k)
            load_x(1, 1)
            sp.wait_ge(w_lo_done, HPC * (OC - RAW) + HPC)
            sp.dma_start(raw[:, 0, 0:D].rearrange("p (e c) -> p e c", e=E), B_v).then_inc(b_load, 16)
            for m in range(MC):
                sp.dma_start(s_col[:, m:m + 1], S_v[m, :, :]).then_inc(s_load, 16)
            sp.dma_start(u_raw[:, :, :], U_v).then_inc(u_load, 16)
            for j in range(2, XSEM):
                load_x(j, j)
            with sp.Fori(1, TILES // XSEM) as i:
                for j in range(XSEM):
                    sp.wait_ge(x_load[j], 16 * i)
                    load_x(XSEM * i + j, j)
            with sp.Fori(0, TILES - 1) as t:
                sp.wait_ge(fin_free, HALF * t + 2 * HALF)
                sp.dma_start(out_v[t, :, :], x_all[:, t, :]).then_inc(stored, 16)
            for n in range(HALF):
                sp.wait_ge(fin_free, HALF * TILES + n + 1)
                cols = slice(n * BANK, (n + 1) * BANK)
                sp.dma_start(out_v[TILES - 1, :, cols], x_all[:, TILES - 1, cols]).then_inc(stored, 16)
            sp.wait_ge(stored, 16 * (TILES - 1 + HALF))

        @block.gpsimd
        def _(pool):
            nc.gpsimd.memset(zeros[:, :].bitcast(F32), 0.0).then_inc(const, 1)
            nc.gpsimd.memset(ident[:, :], 0.0).then_inc(const, 1)
            pool.wait_ge(const, 2)
            nc.gpsimd.affine_select(out=ident[:, :], in_=ident[:, :], compare_op=ALU.not_equal, fill=1.0,
                                    base=0, pattern=[[-1, P]], channel_multiplier=1).then_inc(const, 1)
            for e in range(E):
                nc.gpsimd.memset(iota_e[:, e:e + 1], float(e)).then_inc(const, 1)

            def place_x(t, i, j):
                pool.wait_ge(x_load[j], 16 * i + 16)
                pool.wait_ge(const, 3)
                nc.gpsimd.tensor_copy(x_in[:, j % 2, :], x_all[:, t, :]).then_inc(x_in_ready, 1)

            for j in range(XSEM):
                if j >= 2:
                    pool.wait_ge(xt_done, 2 * (j - 2) + 2)
                place_x(j, 0, j)
            with pool.Fori(1, TILES // XSEM) as i:
                for j in range(XSEM):
                    pool.wait_ge(xt_done, 2 * (XSEM * i + j - 2) + 2)
                    place_x(XSEM * i + j, i, j)

        @block.tensor
        def _(pe):
            def triple(dst, l_hi, l_lo, r_hi, r_lo, first, last, shared=False):
                nc.tensor.matmul(dst, l_hi, r_hi, start=first, stop=False, skip_group_check=shared)
                nc.tensor.matmul(dst, l_hi, r_lo, start=False, stop=False, skip_group_check=shared)
                return nc.tensor.matmul(dst, l_lo, r_hi, start=False, stop=last, skip_group_check=shared)

            def transpose_x(t, q, b):
                if b == 0:
                    pe.wait_ge(x_in_ready, t + 1)
                for c in range(CPB):
                    k = CPB * b + c
                    last = nc.tensor.transpose(tr[b][:, c * P:(c + 1) * P], x_in[:, q, k * P:(k + 1) * P], ident[:, :])
                last.then_inc(xt_done, 1)

            def p_chunk(k, j):
                for m in range(DC):
                    if m % (DC // HPC) == 0:
                        pe.wait_ge(w_lo_done, HPC * k + m // (DC // HPC) + 1)
                    cols = slice(m * P, (m + 1) * P)
                    h = slice(RANK * (m % 2), RANK * (m % 2 + 1))
                    last = triple(p_bank[m // 2][:, h], w_hi[:, j % 2, cols], w_lo[:, j % 2, cols],
                                  v_hi[:, k, :], v_lo[:, k, :], False, True, shared=True)
                    if m % (DC // HPC) == DC // HPC - 1:
                        last.then_inc(w_used, 1)

            def project(t, q, k):
                xk = (xT_hi[:, q, k, :], xT_lo[:, q, k, :])
                return triple(pj[q][:, 0:COLS], *xk, proj_hi[:, k, :], proj_lo[:, k, :], k == 0, k == DC - 1)

            def step(s, q, has_project=True, has_transpose=True, has_mix=True, has_expand=True,
                     transposes=((0, 0), (2, 1)), u_transposes=()):
                first = isinstance(s, int) and s == 0
                if has_project:
                    if not (isinstance(s, int) and s < 2):
                        pe.wait_ge(z_copied, s - 1)
                    for k in range(DC):
                        if k % CPB == 0:
                            pe.wait_ge(xt_lo, 2 * s + k // CPB + 1)
                        if first and k % 2 == 0:
                            pe.wait_ge(*((p_lo, k // 2 + 1) if k < 4 else (fin_free, k // 2 - 1)))
                        last = project(s, q, k)
                        for at, m, b in u_transposes:
                            if at == k:
                                transpose_u(m, b)
                        for at, b in transposes:
                            if at == k and has_transpose:
                                if b == 1:
                                    pe.wait_ge(xt_lo, 2 * s + 2)
                                if isinstance(s, int) and s == 1:
                                    pe.wait_ge(wt_lo, 4 + b + 1)
                                transpose_x(s + 1, 1 - q, b)
                        if has_mix and k == CPB - 1:
                            transpose_gh(s - 1)
                    last.then_inc(pj_done, 1)
                elif has_mix:
                    transpose_gh(s - 1)
                if has_expand and not has_project:
                    pe.wait_ge(zt_lo, s - 1)
                    expand(s - 2, q, 0)
                if has_mix:
                    pe.wait_ge(gt_lo, s)
                    triple(pj[1 - q][:, Z0:COLS], ghT_hi[:, :], ghT_lo[:, :], bv_hi[:, :], bv_lo[:, :],
                           False, True, shared=True).then_inc(z_done, 1)
                if has_expand:
                    if has_project:
                        pe.wait_ge(zt_lo, s - 1)
                        expand(s - 2, q, 0)
                    else:
                        expand(s - 2, q, 1, parts=[0])
                if has_mix:
                    pe.wait_ge(z_copied, s)
                    if not (isinstance(s, int) and s == 1):
                        pe.wait_ge(zt_lo, s - 1)
                    for m in range(MC):
                        last = nc.tensor.transpose(zt[:, m * P:(m + 1) * P], z_sb[:, m * P:(m + 1) * P], ident[:, :])
                    last.then_inc(zt_done, 1)
                if has_expand:
                    expand(s - 2, q, 1, parts=range(MC) if has_project else range(1, MC))

            def transpose_gh(t):
                pe.wait_ge(gh_done, t + 1)
                nc.tensor.transpose(gt[:, 0:P], gh[:, :], ident[:, :]).then_inc(gt_done, 1)

            def expand(t, q, n, parts=range(MC)):
                if 0 in parts:
                    pe.wait_ge(fin_free, HALF * t + n + 1)
                for m in parts:
                    zk = slice(m * P, (m + 1) * P)
                    o = slice(n * BANK, (n + 1) * BANK)
                    last = triple(fin[n][:, :], zT_hi[:, q, zk], zT_lo[:, q, zk], us_hi[:, m, o], us_lo[:, m, o],
                                  m == 0, m == MC - 1)
                    if m == MC - 1:
                        last.then_inc(fin_done, 1)

            def transpose_u(m, b):
                if m == 0 and b == 0:
                    pe.wait_ge(u_load, 16)
                if m == 0:
                    pe.wait_ge(xt_lo, 2 + b + 1)
                else:
                    pe.wait_ge(wt_lo, 2 + b + 1)
                for c in range(CPB):
                    last = nc.tensor.transpose(tr[b][:, c * P:(c + 1) * P],
                                               u_raw[:, CPB * b + c, m * P:(m + 1) * P], ident[:, :])
                last.then_inc(wt_done, 1)

            pe.wait_ge(const, 1)
            zero_row = zeros[:, :].rearrange("p (o n) -> p o n", o=1).to_broadcast([P, CPB, P])
            for n in range(ZERO_ROUNDS):
                for b in range(4):
                    last = nc.tensor.matmul(p_bank[b][:, :].rearrange("p (c n) -> p c n", c=CPB), zeros[:, :],
                                            zero_row, start=True, stop=True)
                    if n == 0:
                        last.then_inc(w_used, 1)
            with pe.Fori(0, OC // RAW) as i:
                for j in range(RAW):
                    p_chunk(RAW * i + j, j)

            pe.wait_ge(const, 3)
            pe.wait_ge(wr_load, 16)
            for k in range(DC):
                last = nc.tensor.transpose(wrT[:, k * E:(k + 1) * E], wr_raw[:, k * P:(k + 1) * P], ident[0:E, 0:E])
            last.then_inc(wr_done, 1)
            pe.wait_ge(a_load, 16)
            for b in range(2):
                for c in range(CPB):
                    k = CPB * b + c
                    last = nc.tensor.transpose(tr[b][:, c * P:(c + 1) * P], a_raw[:, k * P:(k + 1) * P], ident[:, :])
                last.then_inc(wt_done, 1)
            pe.wait_ge(w_lo_done, HPC * OC + 1)
            for k in range(OC):
                cols = slice(k * ER, (k + 1) * ER)
                last = triple(bv_ps, w_hi[:, 0, cols], w_lo[:, 0, cols], v_hi[:, k, :], v_lo[:, k, :],
                              k == 0, k == OC - 1)
                if k in (3, 5):
                    pe.wait_ge(wt_lo, (k - 1) // 2)
                    transpose_x(0, 0, (k - 3) // 2)
            last.then_inc(bv_done, 1)

            step(0, 0, has_mix=False, has_expand=False, u_transposes=((4, 0, 0), (6, 0, 1)))
            pe.wait_ge(bv_lo_done, 1)
            step(1, 1, has_expand=False, transposes=((3, 0), (5, 1)), u_transposes=((0, 1, 0), (1, 1, 1)))
            with pe.Fori(1, TILES // 2 - 1) as i:
                for q in range(2):
                    step(2 * i + q, q)
            step(TILES - 2, 0)
            step(TILES - 1, 1, has_transpose=False)
            step(TILES, 0, has_project=False, has_transpose=False)
            step(TILES + 1, 1, has_project=False, has_transpose=False, has_mix=False)

        @block.scalar
        def _(act):
            def split_x(t, q):
                for b in range(2):
                    act.wait_ge(xt_done, 2 * t + b + 1)
                    nc.scalar.copy(xT_hi[:, q, CPB * b:CPB * (b + 1), :],
                                   tr[b][:, :].rearrange("p (c n) -> p c n", c=CPB)).then_inc(xt_hi, 1)

            def scale_u(m):
                for b in range(2):
                    act.wait_ge(wt_done, 2 + 2 * m + b + 1)
                    nc.scalar.activation(us_hi[:, m, b * BANK:(b + 1) * BANK], tr[b][:, :], ACT.Copy,
                                         scale=s_col[:, m:m + 1]).then_inc(wt_hi, 1)

            def step(s, q, has_project=True, has_transpose=True, has_mix=True, u_chunk=None, u_first=False):
                if u_first:
                    scale_u(u_chunk)
                if has_transpose:
                    split_x(s + 1, 1 - q)
                if u_chunk is not None and not u_first:
                    scale_u(u_chunk)
                if has_mix:
                    act.wait_ge(gt_done, s)
                    nc.scalar.copy(ghT_hi[:, :], gt[:, 0:P]).then_inc(gt_hi, 1)
                    act.wait_ge(z_done, s)
                    nc.scalar.copy(z_sb[:, :], pj[1 - q][:, Z0:COLS]).then_inc(z_copied, 1)
                if has_project:
                    act.wait_ge(dtop_ready, s + 1)
                    nc.scalar.activation(etop[:, :], dtop[:, :], ACT.Exp, accum_out=esum[:, :]).then_inc(exp_done, 1)
                if has_mix:
                    act.wait_ge(zt_done, s)
                    nc.scalar.copy(zT_hi[:, 1 - q, :], zt[:, 0:RANK]).then_inc(zt_hi, 1)

            act.wait_ge(const, 3 + E)
            nc.scalar.activation(esum[:, :], iota_e[:, 0:1], ACT.Exp).then_inc(act_warm, 1)
            act.wait_ge(act_warm, 1)
            with act.Fori(0, OC // RAW) as i:
                for j in range(RAW):
                    k = RAW * i + j
                    act.wait_ge(va_load[j], 32 * i + 32)
                    nc.scalar.copy(v_hi[:, k, :], raw[:, j, D:D + RANK])
                    for h in range(HPC):
                        cols = slice(h * WH, (h + 1) * WH)
                        if h == 1:
                            act.wait_ge(wb_load[j], 16 * i + 16)
                        act.wait_ge(w_used, HPC * k + h + 1)
                        nc.scalar.copy(w_hi[:, j % 2, cols], raw[:, j, cols]).then_inc(w_hi_done, 1)
            act.wait_ge(b_load, 16)
            act.wait_ge(w_used, HPC * OC + HPC)
            nc.scalar.copy(w_hi[:, 0, :].rearrange("p (k e r) -> p k e r", k=OC, e=E),
                           raw[:, 0, 0:D].rearrange("p (e k r) -> p k e r", e=E, k=OC)).then_inc(w_hi_done, 1)
            act.wait_ge(wr_done, 1)
            nc.scalar.copy(proj_hi[:, :, LOG:LOG + E], wrT.rearrange("p (k e) -> p k e", k=DC)).then_inc(wr_hi, 1)
            for b in range(2):
                act.wait_ge(wt_done, b + 1)
                nc.scalar.copy(proj_hi[:, CPB * b:CPB * (b + 1), 0:ER],
                               tr[b][:, :].rearrange("p (c n) -> p c n", c=CPB)).then_inc(wt_hi, 1)
            act.wait_ge(w_used, HPC * OC + 4)
            for b in range(4):
                if b == 1:
                    split_x(0, 0)
                nc.scalar.copy(proj_hi[:, 2 * b:2 * b + 2, Z0:COLS],
                               p_bank[b][:, :].rearrange("p (c n) -> p c n", c=2)).then_inc(p_hi, 1)
            act.wait_ge(bv_done, 1)
            nc.scalar.copy(bv_hi[:, :], bv_ps).then_inc(bv_hi_done, 1)
            act.wait_ge(s_load, 16 * MC)
            step(0, 0, has_mix=False, u_chunk=0)
            step(1, 1, u_chunk=1, u_first=True)
            with act.Fori(1, TILES // 2 - 1) as i:
                for q in range(2):
                    step(2 * i + q, q)
            step(TILES - 2, 0)
            step(TILES - 1, 1, has_transpose=False)
            step(TILES, 0, has_project=False, has_transpose=False)

        @block.vector
        def _(dve):
            def split_x(t, q):
                for b in range(2):
                    dve.wait_ge(xt_hi, 2 * t + b + 1)
                    blocks = slice(CPB * b, CPB * (b + 1))
                    nc.vector.tensor_sub(xT_lo[:, q, blocks, :], tr[b][:, :].rearrange("p (c n) -> p c n", c=CPB),
                                         xT_hi[:, q, blocks, :].bitcast(F32)).then_inc(xt_lo, 1)

            def gates_top(s, q):
                n = GATE_STEPS * s
                dve.wait_ge(pj_done, s + 1)
                nc.vector.scalar_tensor_tensor(logit[:, :], target[:, s, :], LANG_BIAS, pj[q][:, LOG:LOG + E],
                                               ALU.mult, ALU.add).then_inc(gate_step, 1)
                nc.vector.drain()
                nc.vector.max(top[:, :], logit[:, :]).then_inc(gate_step, 1)
                nc.vector.drain()
                nc.vector.tensor_scalar(dtop[:, :], top[:, 0:2], top[:, 0:1], None, ALU.subtract).then_inc(dtop_ready, 1)
                nc.vector.max_index(top_i[:, :], top[:, :], logit[:, :]).then_inc(gate_step, 1)
                dve.wait_ge(gate_step, n + 3)
                nc.vector.tensor_copy(top_f[:, :], top_i[:, 0:2]).then_inc(gate_step, 1)

            def gates_apply(s, q):
                n = GATE_STEPS * s
                dve.wait_ge(exp_done, s + 1)
                nc.vector.reciprocal(rsum[:, :], esum[:, :]).then_inc(gate_step, 1)
                dve.wait_ge(gate_step, n + 5)
                nc.vector.tensor_scalar(wtop[:, :], etop[:, :], rsum[:, :], SCALING, ALU.mult, ALU.mult).then_inc(gate_step, 1)
                dve.wait_ge(gate_step, n + 6)
                for j in range(2):
                    nc.vector.tensor_scalar(pick[:, j, :], iota_e[:, :], top_f[:, j:j + 1], wtop[:, j:j + 1],
                                            ALU.is_equal, ALU.mult).then_inc(gate_step, 1)
                dve.wait_ge(gate_step, n + 8)
                nc.vector.tensor_add(gate[:, :], pick[:, 0, :], pick[:, 1, :]).then_inc(gate_step, 1)
                dve.wait_ge(gate_step, n + 9)
                nc.vector.tensor_tensor(gh[:, :].rearrange("p (e r) -> p e r", e=E),
                                        pj[q][:, 0:ER].rearrange("p (e r) -> p e r", e=E),
                                        gate[:, :].rearrange("p (e o) -> p e o", o=1).to_broadcast([P, E, R]),
                                        ALU.mult).then_inc(gh_done, 1)

            def residual(t, n):
                cols = slice(n * BANK, (n + 1) * BANK)
                dve.wait_ge(fin_done, HALF * t + n + 1)
                nc.vector.tensor_add(x_all[:, t, cols], fin[n][:, :], x_all[:, t, cols]).then_inc(fin_free, 1)

            def scale_u(m):
                for b in range(2):
                    cols = slice(b * BANK, (b + 1) * BANK)
                    dve.wait_ge(wt_hi, 2 + 2 * m + b + 1)
                    nc.vector.scalar_tensor_tensor(us_lo[:, m, cols], tr[b][:, :], s_col[:, m:m + 1],
                                                   us_hi[:, m, cols].bitcast(F32), ALU.mult,
                                                   ALU.subtract).then_inc(wt_lo, 1)

            def step(s, q, has_project=True, has_transpose=True, has_mix=True, has_expand=True, u_chunk=None,
                     u_first=False):
                if u_first:
                    scale_u(u_chunk)
                if has_transpose:
                    split_x(s + 1, 1 - q)
                if u_chunk is not None and not u_first:
                    scale_u(u_chunk)
                if has_mix:
                    dve.wait_ge(gt_hi, s)
                    nc.vector.tensor_sub(ghT_lo[:, :], gt[:, 0:P], ghT_hi[:, :].bitcast(F32)).then_inc(gt_lo, 1)
                if has_project:
                    gates_top(s, q)
                    gates_apply(s, q)
                if has_expand:
                    residual(s - 2, 0)
                if has_mix:
                    dve.wait_ge(zt_hi, s)
                    nc.vector.tensor_sub(zT_lo[:, 1 - q, :], zt[:, 0:RANK],
                                         zT_hi[:, 1 - q, :].bitcast(F32)).then_inc(zt_lo, 1)
                if has_expand:
                    residual(s - 2, 1)

            with dve.Fori(0, OC // RAW) as i:
                for j in range(RAW):
                    k = RAW * i + j
                    for h in range(HPC):
                        cols = slice(h * WH, (h + 1) * WH)
                        dve.wait_ge(w_hi_done, HPC * k + h + 1)
                        if h == 0:
                            nc.vector.tensor_sub(v_lo[:, k, :], raw[:, j, D:D + RANK], v_hi[:, k, :].bitcast(F32))
                        nc.vector.tensor_sub(w_lo[:, j % 2, cols], raw[:, j, cols],
                                             w_hi[:, j % 2, cols].bitcast(F32)).then_inc(w_lo_done, 1)
            dve.wait_ge(ids_load, 16)
            dve.wait_ge(const, 3 + E)
            nc.vector.tensor_copy(ids_f[:, :], ids_i[:, :]).then_inc(setup, 1)
            dve.wait_ge(setup, 1)
            for h in range(2):
                rows = slice(h * SEQ, (h + 1) * SEQ)
                nc.vector.tensor_tensor(
                    target[rows, :, :],
                    ids_f[rows, h:NB:2].rearrange("p (t o) -> p t o", o=1).to_broadcast([SEQ, TILES, E]),
                    iota_e[rows, :].rearrange("p (o e) -> p o e", o=1).to_broadcast([SEQ, TILES, E]),
                    ALU.is_equal).then_inc(setup, 1)
            dve.wait_ge(setup, 3)
            dve.wait_ge(w_hi_done, HPC * OC + 1)
            nc.vector.tensor_sub(w_lo[:, 0, :].rearrange("p (k e r) -> p k e r", k=OC, e=E),
                                 raw[:, 0, 0:D].rearrange("p (e k r) -> p k e r", e=E, k=OC),
                                 w_hi[:, 0, :].bitcast(F32).rearrange("p (k e r) -> p k e r", k=OC, e=E)
                                 ).then_inc(w_lo_done, 1)
            dve.wait_ge(wr_hi, 1)
            nc.vector.tensor_sub(proj_lo[:, :, LOG:LOG + E], wrT.rearrange("p (k e) -> p k e", k=DC),
                                 proj_hi[:, :, LOG:LOG + E].bitcast(F32)).then_inc(wr_lo, 1)
            for b in range(2):
                dve.wait_ge(wt_hi, b + 1)
                blocks = slice(CPB * b, CPB * (b + 1))
                nc.vector.tensor_sub(proj_lo[:, blocks, 0:ER], tr[b][:, :].rearrange("p (c n) -> p c n", c=CPB),
                                     proj_hi[:, blocks, 0:ER].bitcast(F32)).then_inc(wt_lo, 1)
            for b in range(4):
                if b == 1:
                    split_x(0, 0)
                dve.wait_ge(p_hi, b + 1)
                nc.vector.tensor_sub(proj_lo[:, 2 * b:2 * b + 2, Z0:COLS],
                                     p_bank[b][:, :].rearrange("p (c n) -> p c n", c=2),
                                     proj_hi[:, 2 * b:2 * b + 2, Z0:COLS].bitcast(F32)).then_inc(p_lo if b < 2 else fin_free, 1)
            dve.wait_ge(bv_hi_done, 1)
            nc.vector.tensor_sub(bv_lo[:, :], bv_ps, bv_hi[:, :].bitcast(F32)).then_inc(bv_lo_done, 1)
            step(0, 0, has_mix=False, has_expand=False, u_chunk=0)
            step(1, 1, has_expand=False, u_chunk=1, u_first=True)
            with dve.Fori(1, TILES // 2 - 1) as i:
                for q in range(2):
                    step(2 * i + q, q)
            step(TILES - 2, 0)
            step(TILES - 1, 1, has_transpose=False)
            step(TILES, 0, has_project=False, has_transpose=False)
            step(TILES + 1, 1, has_project=False, has_transpose=False, has_mix=False)


INPUTS = ['x', 'itok_B_0_7', 'L0_cond_W', 'L0_cond_Wr', 'L0_cond_A', 'L0_cond_B', 'L0_ffn_U', 'L0_ffn_S', 'L0_ffn_V']


def kernel(**inputs):
    import numpy as np
    import concourse.bacc as bacc
    from concourse.bass_utils import run_bass_kernel_spmd

    nc = bacc.Bacc("TRN2", target_bir_lowering=False, num_devices=1)
    arrays, args = {}, []
    for name in INPUTS:
        a = np.ascontiguousarray(inputs[name])
        arrays["in_" + name] = a
        args.append(nc.dram_tensor("in_" + name, a.shape, mybir.dt.from_np(a.dtype), kind="ExternalInput").ap())
    out = nc.dram_tensor("out", inputs["x"].shape, F32, kind="ExternalOutput")
    adaln_ffn(nc, *args, out.ap())
    result = run_bass_kernel_spmd(nc, [arrays], core_ids=[0])
    return result.results[0]["out"]
```

```python
from contextlib import ExitStack

import concourse.bass as bass
from concourse import mybir

F32 = mybir.dt.float32
F32R = mybir.dt.float32r
I32 = mybir.dt.int32
U32 = mybir.dt.uint32
ALU = mybir.AluOpType
ACT = mybir.ActivationFunctionType

LANG_BIAS = 5.0
SCALING = 32.0 / 16.0


def adaln_ffn(nc, x, ids, W, Wr, A, B, U, S, V, out):
    P = 128
    NB, SEQ, D = x.shape
    E, R, _ = A.shape
    O, RANK = V.shape
    ER = E * R
    TILES = NB * SEQ // P
    DC = D // P
    OC = O // P
    MC = RANK // P
    BANK = 512
    HALF = D // BANK
    CPB = BANK // P
    LOG = ER
    Z0 = ER + E
    COLS = ER + E + RANK
    RAW = 4
    XSEM = 4
    WH = D // 2
    HPC = 2
    ZERO_ROUNDS = 3
    assert ER == P and P % SEQ == 0 and P // SEQ == 2 and O == D and RANK * 2 == BANK
    assert OC == DC and DC == 2 * CPB and OC % RAW == 0 and TILES % XSEM == 0 and COLS <= BANK

    W_v = W.rearrange("(p k) d -> p k d", k=OC)
    V_v = V.rearrange("(p k) r -> p k r", k=OC)
    B_v = B.rearrange("e (p k) r -> p e (k r)", k=OC)
    A_v = A.rearrange("e r d -> (e r) d")
    U_v = U.rearrange("(t p) r -> p t r", p=P)
    S_v = S.rearrange("(m p o) -> m p o", p=P, o=1)
    x_v = x.rearrange("b t d -> (b t) d").rearrange("(g p) d -> g p d", p=P)
    out_v = out.rearrange("b t d -> (b t) d").rearrange("(g p) d -> g p d", p=P)

    with ExitStack() as ctx:
        def sb(name, shape, dt):
            return ctx.enter_context(nc.sbuf_tensor(name, shape, dt))

        def bank(name):
            return ctx.enter_context(nc.psum_tensor(name, [P, BANK], F32))

        def sem(name):
            return ctx.enter_context(nc.semaphore(name))

        x_all = sb("x_all", [P, TILES, D], F32)
        x_in = sb("x_in", [P, 2, D], F32)
        xT_hi = sb("xT_hi", [P, 2, DC, P], F32R)
        xT_lo = sb("xT_lo", [P, 2, DC, P], F32R)
        raw = sb("raw", [P, RAW, D + RANK], F32)
        w_hi = sb("w_hi", [P, 2, D], F32R)
        w_lo = sb("w_lo", [P, 2, D], F32R)
        v_hi = sb("v_hi", [P, OC, RANK], F32R)
        v_lo = sb("v_lo", [P, OC, RANK], F32R)
        proj_hi = sb("proj_hi", [P, DC, COLS], F32R)
        proj_lo = sb("proj_lo", [P, DC, COLS], F32R)
        us_hi = sb("us_hi", [P, MC, O], F32R)
        us_lo = sb("us_lo", [P, MC, O], F32R)
        bv_hi = sb("bv_hi", [P, RANK], F32R)
        bv_lo = sb("bv_lo", [P, RANK], F32R)
        a_raw = sb("a_raw", [P, D], F32)
        wr_raw = sb("wr_raw", [E, D], F32)
        u_raw = sb("u_raw", [P, O // P, RANK], F32)
        s_col = sb("s_col", [P, MC], F32)
        ident = sb("ident", [P, P], F32)
        zeros = sb("zeros", [P, P], F32R)
        ids_i = sb("ids_i", [P, NB], I32)
        ids_f = sb("ids_f", [P, NB], F32)
        iota_e = sb("iota_e", [P, E], F32)
        target = sb("target", [P, TILES, E], F32)
        logit = sb("logit", [P, E], F32)
        top = sb("top", [P, 8], F32)
        top_i = sb("top_i", [P, 8], U32)
        dtop = sb("dtop", [P, 2], F32)
        etop = sb("etop", [P, 2], F32)
        esum = sb("esum", [P, 1], F32)
        rsum = sb("rsum", [P, 1], F32)
        chosen = sb("chosen", [P, 2, E], F32)
        pick = sb("pick", [P, 2, E], F32)
        gate = sb("gate", [P, E], F32)
        gh = sb("gh", [P, ER], F32)
        ghT_hi = sb("ghT_hi", [P, P], F32R)
        ghT_lo = sb("ghT_lo", [P, P], F32R)
        z_sb = sb("z_sb", [P, RANK], F32)
        zT_hi = sb("zT_hi", [P, 2, RANK], F32R)
        zT_lo = sb("zT_lo", [P, 2, RANK], F32R)

        pj = [bank("pj0"), bank("pj1")]
        fin = [bank("fin0"), bank("fin1")]
        tr = [bank("tr0"), bank("tr1")]
        gt = bank("gt")
        zt = bank("zt")
        p_bank = pj + fin
        wrT = gt[:, P:P + DC * E]
        bv_ps = zt[:, RANK:2 * RANK]

        va_load = [sem(f"va_load{j}") for j in range(RAW)]
        wb_load = [sem(f"wb_load{j}") for j in range(RAW)]
        a_load = sem("a_load")
        wr_load = sem("wr_load")
        b_load = sem("b_load")
        u_load = sem("u_load")
        s_load = sem("s_load")
        ids_load = sem("ids_load")
        x_load = [sem(f"x_load{j}") for j in range(XSEM)]
        act_warm = sem("act_warm")
        const = sem("const")
        x_in_ready = sem("x_in_ready")
        setup = sem("setup")
        w_hi_done = sem("w_hi_done")
        v_hi_done = sem("v_hi_done")
        w_lo_done = sem("w_lo_done")
        w_used = sem("w_used")
        p_hi = sem("p_hi")
        p_lo = sem("p_lo")
        wt_done = sem("wt_done")
        wt_hi = sem("wt_hi")
        wt_lo = sem("wt_lo")
        wr_done = sem("wr_done")
        wr_hi = sem("wr_hi")
        bv_done = sem("bv_done")
        bv_hi_done = sem("bv_hi_done")
        bv_lo_done = sem("bv_lo_done")
        xt_done = sem("xt_done")
        xt_hi = sem("xt_hi")
        xt_lo = sem("xt_lo")
        pj_done = sem("pj_done")
        gate_step = sem("gate_step")
        dtop_ready = sem("dtop_ready")
        exp_done = sem("exp_done")
        gh_done = sem("gh_done")
        gt_done = sem("gt_done")
        gt_hi = sem("gt_hi")
        gt_lo = sem("gt_lo")
        z_done = sem("z_done")
        z_copied = sem("z_copied")
        zt_done = sem("zt_done")
        zt_hi = sem("zt_hi")
        zt_lo = sem("zt_lo")
        fin_done = sem("fin_done")
        fin_free = sem("fin_free")
        stored = sem("stored")

        GATE_STEPS = 7

        block = ctx.enter_context(nc.Block())

        @block.sync
        def _(sp):
            def load_w(k):
                if k >= RAW:
                    sp.wait_ge(w_lo_done, HPC * (k - RAW) + HPC)
                sp.dma_start(raw[:, k % RAW, D:D + RANK], V_v[:, k, :]).then_inc(va_load[k % RAW], 16)
                sp.dma_start(raw[:, k % RAW, 0:WH], W_v[:, k, 0:WH]).then_inc(va_load[k % RAW], 16)
                sp.dma_start(raw[:, k % RAW, WH:D], W_v[:, k, WH:D]).then_inc(wb_load[k % RAW], 16)

            def load_x(t, j):
                sp.dma_start(x_all[:, t, :], x_v[t, :, :]).then_inc(x_load[j], 16)

            for k in range(RAW):
                load_w(k)
            sp.dma_start(ids_i[:, :], ids.rearrange("(o n) -> o n", o=1).to_broadcast([P, NB])).then_inc(ids_load, 16)
            sp.dma_start(a_raw[:, :], A_v).then_inc(a_load, 16)
            sp.dma_start(wr_raw[:, :], Wr).then_inc(wr_load, 16)
            load_x(0, 0)
            for k in range(RAW, OC):
                load_w(k)
            load_x(1, 1)
            sp.wait_ge(w_lo_done, HPC * (OC - RAW) + HPC)
            sp.dma_start(raw[:, 0, 0:D].rearrange("p (e c) -> p e c", e=E), B_v).then_inc(b_load, 16)
            for m in range(MC):
                sp.dma_start(s_col[:, m:m + 1], S_v[m, :, :]).then_inc(s_load, 16)
            sp.dma_start(u_raw[:, :, :], U_v).then_inc(u_load, 16)
            for j in range(2, XSEM):
                load_x(j, j)
            with sp.Fori(1, TILES // XSEM) as i:
                for j in range(XSEM):
                    sp.wait_ge(x_load[j], 16 * i)
                    load_x(XSEM * i + j, j)
            with sp.Fori(0, TILES - 1) as t:
                sp.wait_ge(fin_free, HALF * t + 2 * HALF)
                sp.dma_start(out_v[t, :, :], x_all[:, t, :]).then_inc(stored, 16)
            for n in range(HALF):
                sp.wait_ge(fin_free, HALF * TILES + n + 1)
                cols = slice(n * BANK, (n + 1) * BANK)
                sp.dma_start(out_v[TILES - 1, :, cols], x_all[:, TILES - 1, cols]).then_inc(stored, 16)
            sp.wait_ge(stored, 16 * (TILES - 1 + HALF))

        @block.gpsimd
        def _(pool):
            nc.gpsimd.memset(zeros[:, :].bitcast(F32), 0.0).then_inc(const, 1)
            nc.gpsimd.memset(ident[:, :], 0.0).then_inc(const, 1)
            pool.wait_ge(const, 2)
            nc.gpsimd.affine_select(out=ident[:, :], in_=ident[:, :], compare_op=ALU.not_equal, fill=1.0,
                                    base=0, pattern=[[-1, P]], channel_multiplier=1).then_inc(const, 1)
            for e in range(E):
                nc.gpsimd.memset(iota_e[:, e:e + 1], float(e)).then_inc(const, 1)

            def place_x(t, i, j):
                pool.wait_ge(x_load[j], 16 * i + 16)
                pool.wait_ge(const, 3)
                nc.gpsimd.tensor_copy(x_in[:, j % 2, :], x_all[:, t, :]).then_inc(x_in_ready, 1)

            for j in range(XSEM):
                if j >= 2:
                    pool.wait_ge(xt_done, 2 * (j - 2) + 2)
                place_x(j, 0, j)
            with pool.Fori(1, TILES // XSEM) as i:
                for j in range(XSEM):
                    pool.wait_ge(xt_done, 2 * (XSEM * i + j - 2) + 2)
                    place_x(XSEM * i + j, i, j)

        @block.tensor
        def _(pe):
            def triple(dst, l_hi, l_lo, r_hi, r_lo, first, last, shared=False):
                nc.tensor.matmul(dst, l_hi, r_hi, start=first, stop=False, skip_group_check=shared)
                nc.tensor.matmul(dst, l_hi, r_lo, start=False, stop=False, skip_group_check=shared)
                return nc.tensor.matmul(dst, l_lo, r_hi, start=False, stop=last, skip_group_check=shared)

            def transpose_x(t, q, b):
                if b == 0:
                    pe.wait_ge(x_in_ready, t + 1)
                for c in range(CPB):
                    k = CPB * b + c
                    last = nc.tensor.transpose(tr[b][:, c * P:(c + 1) * P], x_in[:, q, k * P:(k + 1) * P], ident[:, :])
                last.then_inc(xt_done, 1)

            def p_chunk(k, j):
                for m in range(DC):
                    if m % (DC // HPC) == 0:
                        pe.wait_ge(w_lo_done, HPC * k + m // (DC // HPC) + 1)
                    cols = slice(m * P, (m + 1) * P)
                    h = slice(RANK * (m % 2), RANK * (m % 2 + 1))
                    last = triple(p_bank[m // 2][:, h], w_hi[:, j % 2, cols], w_lo[:, j % 2, cols],
                                  v_hi[:, k, :], v_lo[:, k, :], False, True, shared=True)
                    if m % (DC // HPC) == DC // HPC - 1:
                        last.then_inc(w_used, 1)

            def project(t, q, k):
                xk = (xT_hi[:, q, k, :], xT_lo[:, q, k, :])
                return triple(pj[q][:, 0:COLS], *xk, proj_hi[:, k, :], proj_lo[:, k, :], k == 0, k == DC - 1)

            def step(s, q, has_project=True, has_transpose=True, has_mix=True, has_expand=True,
                     transposes=((0, 0), (2, 1)), u_transposes=(), gh_at=3, mix_at=5):
                first = isinstance(s, int) and s == 0
                second = isinstance(s, int) and s == 1
                if has_project:
                    if not (isinstance(s, int) and s < 2):
                        pe.wait_ge(z_copied, s - 1)
                    for k in range(DC):
                        if k % CPB == 0:
                            pe.wait_ge(xt_lo, 2 * s + k // CPB + 1)
                        if first and k in (0, 2):
                            pe.wait_ge(p_lo, k // 2 + 1)
                        if first and k in (4, 6):
                            pe.wait_ge(fin_free, k // 2 - 1)
                        last = project(s, q, k)
                        for at, m, b in u_transposes:
                            if at == k:
                                transpose_u(m, b)
                        for at, b in transposes:
                            if at == k and has_transpose:
                                if b == 1:
                                    pe.wait_ge(xt_lo, 2 * s + 2)
                                if not first:
                                    pe.wait_ge(wt_lo, 2 + (0 if second else 2 * MC - 2) + b + 1)
                                transpose_x(s + 1, 1 - q, b)
                        if has_mix and k == gh_at:
                            transpose_gh(s - 1)
                        if has_mix and k == mix_at:
                            mix(s - 1, 1 - q)
                    last.then_inc(pj_done, 1)
                if has_mix:
                    transpose_z(s - 1)
                if has_expand:
                    for n in range(HALF):
                        expand(s - 2, q, n)

            def mix(t, q):
                pe.wait_ge(gt_lo, t + 1)
                triple(pj[q][:, Z0:COLS], ghT_hi[:, :], ghT_lo[:, :], bv_hi[:, :], bv_lo[:, :],
                       False, True, shared=True).then_inc(z_done, 1)

            def transpose_z(t):
                pe.wait_ge(z_copied, t + 1)
                if not (isinstance(t, int) and t == 0):
                    pe.wait_ge(zt_lo, t)
                for m in range(MC):
                    last = nc.tensor.transpose(zt[:, m * P:(m + 1) * P], z_sb[:, m * P:(m + 1) * P], ident[:, :])
                last.then_inc(zt_done, 1)

            def transpose_gh(t):
                pe.wait_ge(gh_done, t + 1)
                nc.tensor.transpose(gt[:, 0:P], gh[:, :], ident[:, :]).then_inc(gt_done, 1)

            def expand(t, q, n, parts=range(MC)):
                if 0 in parts:
                    pe.wait_ge(zt_lo, t + 1)
                    pe.wait_ge(fin_free, HALF * t + n + 1)
                for m in parts:
                    zk = slice(m * P, (m + 1) * P)
                    o = slice(n * BANK, (n + 1) * BANK)
                    last = triple(fin[n][:, :], zT_hi[:, q, zk], zT_lo[:, q, zk], us_hi[:, m, o], us_lo[:, m, o],
                                  m == 0, m == MC - 1)
                    if m == MC - 1:
                        last.then_inc(fin_done, 1)

            def transpose_u(m, b):
                if m == 0 and b == 0:
                    pe.wait_ge(u_load, 16)
                pe.wait_ge(xt_lo, 2 * m + 2 + b + 1)
                for c in range(CPB):
                    last = nc.tensor.transpose(tr[b][:, c * P:(c + 1) * P],
                                               u_raw[:, CPB * b + c, m * P:(m + 1) * P], ident[:, :])
                last.then_inc(wt_done, 1)

            pe.wait_ge(const, 1)
            zero_row = zeros[:, :].rearrange("p (o n) -> p o n", o=1).to_broadcast([P, CPB, P])
            for n in range(ZERO_ROUNDS):
                for b in range(4):
                    last = nc.tensor.matmul(p_bank[b][:, :].rearrange("p (c n) -> p c n", c=CPB), zeros[:, :],
                                            zero_row, start=True, stop=True)
                    if n == 0:
                        last.then_inc(w_used, 1)
            with pe.Fori(0, OC // RAW) as i:
                for j in range(RAW):
                    p_chunk(RAW * i + j, j)

            pe.wait_ge(const, 3)
            pe.wait_ge(wr_load, 16)
            for k in range(DC):
                last = nc.tensor.transpose(wrT[:, k * E:(k + 1) * E], wr_raw[:, k * P:(k + 1) * P], ident[0:E, 0:E])
            last.then_inc(wr_done, 1)
            pe.wait_ge(a_load, 16)
            for b in range(2):
                for c in range(CPB):
                    k = CPB * b + c
                    last = nc.tensor.transpose(tr[b][:, c * P:(c + 1) * P], a_raw[:, k * P:(k + 1) * P], ident[:, :])
                last.then_inc(wt_done, 1)
            pe.wait_ge(w_lo_done, HPC * OC + 1)
            for k in range(OC):
                cols = slice(k * ER, (k + 1) * ER)
                last = triple(bv_ps, w_hi[:, 0, cols], w_lo[:, 0, cols], v_hi[:, k, :], v_lo[:, k, :],
                              k == 0, k == OC - 1)
                if k in (3, 5):
                    pe.wait_ge(wt_lo, (k - 1) // 2)
                    transpose_x(0, 0, (k - 3) // 2)
            last.then_inc(bv_done, 1)

            step(0, 0, has_mix=False, has_expand=False, transposes=((0, 0), (1, 1)),
                 u_transposes=((4, 0, 0), (5, 0, 1)))
            pe.wait_ge(bv_lo_done, 1)
            step(1, 1, has_expand=False, u_transposes=((4, 1, 0), (6, 1, 1)))
            with pe.Fori(1, TILES // 2 - 1) as i:
                for q in range(2):
                    step(2 * i + q, q)
            step(TILES - 2, 0)
            step(TILES - 1, 1, has_transpose=False)
            expand(TILES - 2, 0, 0, parts=[0])
            transpose_gh(TILES - 1)
            expand(TILES - 2, 0, 0, parts=[1])
            mix(TILES - 1, 1)
            expand(TILES - 2, 0, 1, parts=[0])
            transpose_z(TILES - 1)
            expand(TILES - 2, 0, 1, parts=[1])
            for n in range(HALF):
                expand(TILES - 1, 1, n)

        @block.scalar
        def _(act):
            def split_x(t, q, halves=range(2)):
                for b in halves:
                    act.wait_ge(xt_done, 2 * t + b + 1)
                    nc.scalar.copy(xT_hi[:, q, CPB * b:CPB * (b + 1), :],
                                   tr[b][:, :].rearrange("p (c n) -> p c n", c=CPB)).then_inc(xt_hi, 1)

            def scale_u(m, b):
                act.wait_ge(wt_done, 2 + 2 * m + b + 1)
                nc.scalar.activation(us_hi[:, m, b * BANK:(b + 1) * BANK], tr[b][:, :], ACT.Copy,
                                     scale=s_col[:, m:m + 1]).then_inc(wt_hi, 1)

            def step(s, q, has_project=True, has_transpose=True, has_mix=True, with_u=False):
                if has_transpose:
                    split_x(s + 1, 1 - q, [0])
                if has_mix:
                    act.wait_ge(gt_done, s)
                    nc.scalar.copy(ghT_hi[:, :], gt[:, 0:P]).then_inc(gt_hi, 1)
                if has_transpose:
                    split_x(s + 1, 1 - q, [1])
                if with_u:
                    scale_u(s, 0)
                if has_mix:
                    act.wait_ge(z_done, s)
                    nc.scalar.copy(z_sb[:, :], pj[1 - q][:, Z0:COLS]).then_inc(z_copied, 1)
                if with_u:
                    scale_u(s, 1)
                if has_mix:
                    act.wait_ge(zt_done, s)
                    nc.scalar.copy(zT_hi[:, 1 - q, :], zt[:, 0:RANK]).then_inc(zt_hi, 1)
                if has_project:
                    act.wait_ge(dtop_ready, s + 1)
                    nc.scalar.activation(etop[:, :], dtop[:, :], ACT.Exp, accum_out=esum[:, :]).then_inc(exp_done, 1)

            act.wait_ge(const, 3 + E)
            nc.scalar.activation(esum[:, :], iota_e[:, 0:1], ACT.Exp).then_inc(act_warm, 1)
            act.wait_ge(act_warm, 1)
            with act.Fori(0, OC // RAW) as i:
                for j in range(RAW):
                    k = RAW * i + j
                    act.wait_ge(va_load[j], 32 * i + 32)
                    for h in range(HPC):
                        cols = slice(h * WH, (h + 1) * WH)
                        if h == 1:
                            act.wait_ge(wb_load[j], 16 * i + 16)
                        act.wait_ge(w_used, HPC * k + h + 1)
                        nc.scalar.copy(w_hi[:, j % 2, cols], raw[:, j, cols]).then_inc(w_hi_done, 1)
                        if h == 0:
                            nc.scalar.copy(v_hi[:, k, :], raw[:, j, D:D + RANK]).then_inc(v_hi_done, 1)
            act.wait_ge(b_load, 16)
            act.wait_ge(w_used, HPC * OC + HPC)
            nc.scalar.copy(w_hi[:, 0, :].rearrange("p (k e r) -> p k e r", k=OC, e=E),
                           raw[:, 0, 0:D].rearrange("p (e k r) -> p k e r", e=E, k=OC)).then_inc(w_hi_done, 1)
            act.wait_ge(wr_done, 1)
            nc.scalar.copy(proj_hi[:, :, LOG:LOG + E], wrT.rearrange("p (k e) -> p k e", k=DC)).then_inc(wr_hi, 1)
            for b in range(2):
                act.wait_ge(wt_done, b + 1)
                nc.scalar.copy(proj_hi[:, CPB * b:CPB * (b + 1), 0:ER],
                               tr[b][:, :].rearrange("p (c n) -> p c n", c=CPB)).then_inc(wt_hi, 1)
            act.wait_ge(w_used, HPC * OC + 4)
            for b in range(4):
                if b == 1:
                    split_x(0, 0)
                nc.scalar.copy(proj_hi[:, 2 * b:2 * b + 2, Z0:COLS],
                               p_bank[b][:, :].rearrange("p (c n) -> p c n", c=2)).then_inc(p_hi, 1)
            act.wait_ge(bv_done, 1)
            nc.scalar.activation(bv_hi[:, :], bv_ps, ACT.Copy, scale=SCALING).then_inc(bv_hi_done, 1)
            act.wait_ge(s_load, 16 * MC)
            step(0, 0, has_mix=False, with_u=True)
            step(1, 1, with_u=True)
            with act.Fori(1, TILES // 2 - 1) as i:
                for q in range(2):
                    step(2 * i + q, q)
            step(TILES - 2, 0)
            step(TILES - 1, 1, has_transpose=False)
            step(TILES, 0, has_project=False, has_transpose=False)

        @block.vector
        def _(dve):
            def split_x(t, q, halves=range(2)):
                for b in halves:
                    dve.wait_ge(xt_hi, 2 * t + b + 1)
                    blocks = slice(CPB * b, CPB * (b + 1))
                    nc.vector.tensor_sub(xT_lo[:, q, blocks, :], tr[b][:, :].rearrange("p (c n) -> p c n", c=CPB),
                                         xT_hi[:, q, blocks, :].bitcast(F32)).then_inc(xt_lo, 1)

            def gates_top(s, q):
                n = GATE_STEPS * s
                dve.wait_ge(pj_done, s + 1)
                nc.vector.scalar_tensor_tensor(logit[:, :], target[:, s, :], LANG_BIAS, pj[q][:, LOG:LOG + E],
                                               ALU.mult, ALU.add).then_inc(gate_step, 1)
                nc.vector.drain()
                nc.vector.max(top[:, :], logit[:, :]).then_inc(gate_step, 1)
                nc.vector.drain()
                nc.vector.tensor_scalar(dtop[:, :], top[:, 0:2], top[:, 0:1], None, ALU.subtract).then_inc(dtop_ready, 1)
                nc.vector.max_index(top_i[:, :], top[:, :], logit[:, :]).then_inc(gate_step, 1)
                dve.wait_ge(gate_step, n + 3)
                nc.vector.tensor_tensor(chosen[:, :, :],
                                        iota_e[:, :].rearrange("p (o e) -> p o e", o=1).to_broadcast([P, 2, E]),
                                        top_i[:, 0:2].rearrange("p (j o) -> p j o", o=1).to_broadcast([P, 2, E]),
                                        ALU.is_equal).then_inc(gate_step, 1)

            def gates_apply(s, q):
                n = GATE_STEPS * s
                dve.wait_ge(exp_done, s + 1)
                nc.vector.reciprocal(rsum[:, :], esum[:, :]).then_inc(gate_step, 1)
                dve.wait_ge(gate_step, n + 4)
                nc.vector.tensor_tensor(pick[:, :, :], chosen[:, :, :],
                                        etop[:, :].rearrange("p (j o) -> p j o", o=1).to_broadcast([P, 2, E]),
                                        ALU.mult).then_inc(gate_step, 1)
                dve.wait_ge(gate_step, n + 6)
                nc.vector.tensor_add(gate[:, :], pick[:, 0, :], pick[:, 1, :]).then_inc(gate_step, 1)
                dve.wait_ge(gate_step, n + 7)
                nc.vector.scalar_tensor_tensor(gh[:, :].rearrange("p (e r) -> p e r", e=E),
                                               pj[q][:, 0:ER].rearrange("p (e r) -> p e r", e=E), rsum[:, :],
                                               gate[:, :].rearrange("p (e o) -> p e o", o=1).to_broadcast([P, E, R]),
                                               ALU.mult, ALU.mult).then_inc(gh_done, 1)

            def residual(t, n):
                cols = slice(n * BANK, (n + 1) * BANK)
                dve.wait_ge(fin_done, HALF * t + n + 1)
                nc.vector.tensor_add(x_all[:, t, cols], fin[n][:, :], x_all[:, t, cols]).then_inc(fin_free, 1)

            def scale_u(m):
                for b in range(2):
                    cols = slice(b * BANK, (b + 1) * BANK)
                    dve.wait_ge(wt_hi, 2 + 2 * m + b + 1)
                    nc.vector.scalar_tensor_tensor(us_lo[:, m, cols], tr[b][:, :], s_col[:, m:m + 1],
                                                   us_hi[:, m, cols].bitcast(F32), ALU.mult,
                                                   ALU.subtract).then_inc(wt_lo, 1)

            def step(s, q, has_project=True, has_transpose=True, has_mix=True, has_expand=True, with_u=False):
                if has_transpose:
                    split_x(s + 1, 1 - q, [0])
                if has_mix:
                    dve.wait_ge(gt_hi, s)
                    nc.vector.tensor_sub(ghT_lo[:, :], gt[:, 0:P], ghT_hi[:, :].bitcast(F32)).then_inc(gt_lo, 1)
                if has_transpose:
                    split_x(s + 1, 1 - q, [1])
                if with_u:
                    scale_u(s)
                if has_project:
                    gates_top(s, q)
                    gates_apply(s, q)
                if has_expand:
                    residual(s - 2, 0)
                if has_mix:
                    dve.wait_ge(zt_hi, s)
                    nc.vector.tensor_sub(zT_lo[:, 1 - q, :], zt[:, 0:RANK],
                                         zT_hi[:, 1 - q, :].bitcast(F32)).then_inc(zt_lo, 1)
                if has_expand:
                    residual(s - 2, 1)

            with dve.Fori(0, OC // RAW) as i:
                for j in range(RAW):
                    k = RAW * i + j
                    for h in range(HPC):
                        cols = slice(h * WH, (h + 1) * WH)
                        dve.wait_ge(w_hi_done, HPC * k + h + 1)
                        last = nc.vector.tensor_sub(w_lo[:, j % 2, cols], raw[:, j, cols],
                                                    w_hi[:, j % 2, cols].bitcast(F32))
                        if h == 0:
                            dve.wait_ge(v_hi_done, k + 1)
                            last = nc.vector.tensor_sub(v_lo[:, k, :], raw[:, j, D:D + RANK],
                                                        v_hi[:, k, :].bitcast(F32))
                        last.then_inc(w_lo_done, 1)
            dve.wait_ge(ids_load, 16)
            dve.wait_ge(const, 3 + E)
            nc.vector.tensor_copy(ids_f[:, :], ids_i[:, :]).then_inc(setup, 1)
            dve.wait_ge(setup, 1)
            for h in range(2):
                rows = slice(h * SEQ, (h + 1) * SEQ)
                nc.vector.tensor_tensor(
                    target[rows, :, :],
                    ids_f[rows, h:NB:2].rearrange("p (t o) -> p t o", o=1).to_broadcast([SEQ, TILES, E]),
                    iota_e[rows, :].rearrange("p (o e) -> p o e", o=1).to_broadcast([SEQ, TILES, E]),
                    ALU.is_equal).then_inc(setup, 1)
            dve.wait_ge(setup, 3)
            dve.wait_ge(w_hi_done, HPC * OC + 1)
            nc.vector.tensor_sub(w_lo[:, 0, :].rearrange("p (k e r) -> p k e r", k=OC, e=E),
                                 raw[:, 0, 0:D].rearrange("p (e k r) -> p k e r", e=E, k=OC),
                                 w_hi[:, 0, :].bitcast(F32).rearrange("p (k e r) -> p k e r", k=OC, e=E)
                                 ).then_inc(w_lo_done, 1)
            dve.wait_ge(wr_hi, 1)
            nc.vector.tensor_sub(proj_lo[:, :, LOG:LOG + E], wrT.rearrange("p (k e) -> p k e", k=DC),
                                 proj_hi[:, :, LOG:LOG + E].bitcast(F32))
            for b in range(2):
                dve.wait_ge(wt_hi, b + 1)
                blocks = slice(CPB * b, CPB * (b + 1))
                nc.vector.tensor_sub(proj_lo[:, blocks, 0:ER], tr[b][:, :].rearrange("p (c n) -> p c n", c=CPB),
                                     proj_hi[:, blocks, 0:ER].bitcast(F32)).then_inc(wt_lo, 1)
            for b in range(4):
                if b == 1:
                    split_x(0, 0)
                dve.wait_ge(p_hi, b + 1)
                nc.vector.tensor_sub(proj_lo[:, 2 * b:2 * b + 2, Z0:COLS],
                                     p_bank[b][:, :].rearrange("p (c n) -> p c n", c=2),
                                     proj_hi[:, 2 * b:2 * b + 2, Z0:COLS].bitcast(F32)).then_inc(p_lo if b < 2 else fin_free, 1)
            dve.wait_ge(bv_hi_done, 1)
            nc.vector.scalar_tensor_tensor(bv_lo[:, :], bv_ps, SCALING, bv_hi[:, :].bitcast(F32),
                                           ALU.mult, ALU.subtract).then_inc(bv_lo_done, 1)
            step(0, 0, has_mix=False, has_expand=False, with_u=True)
            step(1, 1, has_expand=False, with_u=True)
            with dve.Fori(1, TILES // 2 - 1) as i:
                for q in range(2):
                    step(2 * i + q, q)
            step(TILES - 2, 0)
            step(TILES - 1, 1, has_transpose=False)
            step(TILES, 0, has_project=False, has_transpose=False)
            step(TILES + 1, 1, has_project=False, has_transpose=False, has_mix=False)


INPUTS = ['x', 'itok_B_0_7', 'L0_cond_W', 'L0_cond_Wr', 'L0_cond_A', 'L0_cond_B', 'L0_ffn_U', 'L0_ffn_S', 'L0_ffn_V']


def kernel(**inputs):
    import numpy as np
    import concourse.bacc as bacc
    from concourse.bass_utils import run_bass_kernel_spmd

    nc = bacc.Bacc("TRN2", target_bir_lowering=False, num_devices=1)
    arrays, args = {}, []
    for name in INPUTS:
        a = np.ascontiguousarray(inputs[name])
        arrays["in_" + name] = a
        args.append(nc.dram_tensor("in_" + name, a.shape, mybir.dt.from_np(a.dtype), kind="ExternalInput").ap())
    out = nc.dram_tensor("out", inputs["x"].shape, F32, kind="ExternalOutput")
    adaln_ffn(nc, *args, out.ap())
    result = run_bass_kernel_spmd(nc, [arrays], core_ids=[0])
    return result.results[0]["out"]
```
